# Optimizing a Trainium2 kernel written in Bass

```python
import numpy as np
import jax
import jax.numpy as jnp

def _softmax(x, axis=-1):
    return jax.nn.softmax(x, axis=axis)

def _gelu(x):
    return jax.nn.gelu(x, approximate=True)

def _silu(x):
    return jax.nn.silu(x)

def _sigmoid(x):
    return jax.nn.sigmoid(x)

def _layernorm(x, axis=-1, eps=1e-05):
    m = jnp.mean(x, axis=axis, keepdims=True)
    v = jnp.var(x, axis=axis, keepdims=True)
    return (x - m) / jnp.sqrt(v + eps)

def _scatter_add(tgt, idx, src, axis=0):
    return tgt.at[idx].add(src)

def _segment_sum(src, seg, n):
    return jax.ops.segment_sum(src, seg, n)
kernel_name = 'mk_dlrm_tower_d1_rec_r8_dbd913'

def setup_inputs(seed: int=0):
    np.random.seed(seed)
    _w = jnp.asarray

    def _rec_inputs():
        import jax
        import jax.numpy as jnp
        _tk = jax.random.key(seed)
        ids = jnp.stack([jax.random.randint(jax.random.fold_in(_tk, 200 + f), (2048,), 0, v, jnp.int32) for f, v in enumerate([12500, 1250, 12500, 125000, 12500, 12500, 1000, 12500, 1000, 1250, 12500, 1000, 1000, 1000, 1000, 1250, 1250, 1250, 1250, 1250, 1250, 1000, 1000, 1250, 1000, 1000])], axis=1)
        tbl_0 = 0.05 * jax.random.normal(jax.random.fold_in(_tk, 500 + 0), (12500, 128), jnp.float32)
        tbl_1 = 0.05 * jax.random.normal(jax.random.fold_in(_tk, 500 + 1), (1250, 128), jnp.float32)
        tbl_2 = 0.05 * jax.random.normal(jax.random.fold_in(_tk, 500 + 2), (12500, 128), jnp.float32)
        tbl_3 = 0.05 * jax.random.normal(jax.random.fold_in(_tk, 500 + 3), (125000, 128), jnp.float32)
        tbl_4 = 0.05 * jax.random.normal(jax.random.fold_in(_tk, 500 + 4), (12500, 128), jnp.float32)
        tbl_5 = 0.05 * jax.random.normal(jax.random.fold_in(_tk, 500 + 5), (12500, 128), jnp.float32)
        tbl_6 = 0.05 * jax.random.normal(jax.random.fold_in(_tk, 500 + 6), (1000, 128), jnp.float32)
        tbl_7 = 0.05 * jax.random.normal(jax.random.fold_in(_tk, 500 + 7), (12500, 128), jnp.float32)
        tbl_8 = 0.05 * jax.random.normal(jax.random.fold_in(_tk, 500 + 8), (1000, 128), jnp.float32)
        tbl_9 = 0.05 * jax.random.normal(jax.random.fold_in(_tk, 500 + 9), (1250, 128), jnp.float32)
        tbl_10 = 0.05 * jax.random.normal(jax.random.fold_in(_tk, 500 + 10), (12500, 128), jnp.float32)
        tbl_11 = 0.05 * jax.random.normal(jax.random.fold_in(_tk, 500 + 11), (1000, 128), jnp.float32)
        tbl_12 = 0.05 * jax.random.normal(jax.random.fold_in(_tk, 500 + 12), (1000, 128), jnp.float32)
        tbl_13 = 0.05 * jax.random.normal(jax.random.fold_in(_tk, 500 + 13), (1000, 128), jnp.float32)
        tbl_14 = 0.05 * jax.random.normal(jax.random.fold_in(_tk, 500 + 14), (1000, 128), jnp.float32)
        tbl_15 = 0.05 * jax.random.normal(jax.random.fold_in(_tk, 500 + 15), (1250, 128), jnp.float32)
        tbl_16 = 0.05 * jax.random.normal(jax.random.fold_in(_tk, 500 + 16), (1250, 128), jnp.float32)
        tbl_17 = 0.05 * jax.random.normal(jax.random.fold_in(_tk, 500 + 17), (1250, 128), jnp.float32)
        tbl_18 = 0.05 * jax.random.normal(jax.random.fold_in(_tk, 500 + 18), (1250, 128), jnp.float32)
        tbl_19 = 0.05 * jax.random.normal(jax.random.fold_in(_tk, 500 + 19), (1250, 128), jnp.float32)
        tbl_20 = 0.05 * jax.random.normal(jax.random.fold_in(_tk, 500 + 20), (1250, 128), jnp.float32)
        tbl_21 = 0.05 * jax.random.normal(jax.random.fold_in(_tk, 500 + 21), (1000, 128), jnp.float32)
        tbl_22 = 0.05 * jax.random.normal(jax.random.fold_in(_tk, 500 + 22), (1000, 128), jnp.float32)
        tbl_23 = 0.05 * jax.random.normal(jax.random.fold_in(_tk, 500 + 23), (1250, 128), jnp.float32)
        tbl_24 = 0.05 * jax.random.normal(jax.random.fold_in(_tk, 500 + 24), (1000, 128), jnp.float32)
        tbl_25 = 0.05 * jax.random.normal(jax.random.fold_in(_tk, 500 + 25), (1000, 128), jnp.float32)
        _rk = jax.random.fold_in(_tk, 7)
        r_dense_x = -0.000514642 + 1.00011 * jax.random.normal(jax.random.fold_in(_rk, 101), (2048, 128), jnp.float32)
        W_top1 = 0.0456912 * jax.random.normal(jax.random.fold_in(_tk, 801), (479, 512), jnp.float32)
        W_top2 = 0.0441942 * jax.random.normal(jax.random.fold_in(_tk, 802), (512, 256), jnp.float32)
        W_top3 = 0.0625 * jax.random.normal(jax.random.fold_in(_tk, 803), (256, 1), jnp.float32)
        b_top1 = jnp.zeros((512,), jnp.float32)
        b_top2 = jnp.zeros((256,), jnp.float32)
        return (r_dense_x, ids, tbl_0, tbl_1, tbl_2, tbl_3, tbl_4, tbl_5, tbl_6, tbl_7, tbl_8, tbl_9, tbl_10, tbl_11, tbl_12, tbl_13, tbl_14, tbl_15, tbl_16, tbl_17, tbl_18, tbl_19, tbl_20, tbl_21, tbl_22, tbl_23, tbl_24, tbl_25, W_top1, b_top1, W_top2, b_top2, W_top3)
    r_dense_x, ids, tbl_0, tbl_1, tbl_2, tbl_3, tbl_4, tbl_5, tbl_6, tbl_7, tbl_8, tbl_9, tbl_10, tbl_11, tbl_12, tbl_13, tbl_14, tbl_15, tbl_16, tbl_17, tbl_18, tbl_19, tbl_20, tbl_21, tbl_22, tbl_23, tbl_24, tbl_25, W_top1, b_top1, W_top2, b_top2, W_top3 = _rec_inputs()

    def _L0_rec_setup():
        import jax, jax.numpy as jnp
        import numpy as np
        F = 26
        D = 128
        B = 2048
        _TRIU_I, _TRIU_J = np.triu_indices(F + 1, k=1)
        _TRIU_I = jnp.asarray(_TRIU_I)
        _TRIU_J = jnp.asarray(_TRIU_J)
        key = jax.random.key(seed)
        k1, k2 = jax.random.split(key)
        sparse_x = jax.random.normal(k1, (B, F, D), dtype=jnp.float32)
        dense_x = jax.random.normal(k2, (B, D), dtype=jnp.float32)
        return {'sparse_x': sparse_x, 'dense_x': dense_x}
    _L0_rec_all = _L0_rec_setup()
    _L0_rec_in = {k: v for k, v in _L0_rec_all.items() if k in ()}
    del _L0_rec_all
    return {'r_dense_x': r_dense_x, 'ids': ids, 'tbl_0': tbl_0, 'tbl_1': tbl_1, 'tbl_2': tbl_2, 'tbl_3': tbl_3, 'tbl_4': tbl_4, 'tbl_5': tbl_5, 'tbl_6': tbl_6, 'tbl_7': tbl_7, 'tbl_8': tbl_8, 'tbl_9': tbl_9, 'tbl_10': tbl_10, 'tbl_11': tbl_11, 'tbl_12': tbl_12, 'tbl_13': tbl_13, 'tbl_14': tbl_14, 'tbl_15': tbl_15, 'tbl_16': tbl_16, 'tbl_17': tbl_17, 'tbl_18': tbl_18, 'tbl_19': tbl_19, 'tbl_20': tbl_20, 'tbl_21': tbl_21, 'tbl_22': tbl_22, 'tbl_23': tbl_23, 'tbl_24': tbl_24, 'tbl_25': tbl_25, 'W_top1': W_top1, 'b_top1': b_top1, 'W_top2': W_top2, 'b_top2': b_top2, 'W_top3': W_top3}

def reference(r_dense_x, ids, tbl_0, tbl_1, tbl_2, tbl_3, tbl_4, tbl_5, tbl_6, tbl_7, tbl_8, tbl_9, tbl_10, tbl_11, tbl_12, tbl_13, tbl_14, tbl_15, tbl_16, tbl_17, tbl_18, tbl_19, tbl_20, tbl_21, tbl_22, tbl_23, tbl_24, tbl_25, W_top1, b_top1, W_top2, b_top2, W_top3):
    import jax
    import jax.numpy as jnp

    def _L0_rec_ref(sparse_x, dense_x):
        import jax, jax.numpy as jnp
        import numpy as np
        F = 26
        D = 128
        B = 2048
        _TRIU_I, _TRIU_J = np.triu_indices(F + 1, k=1)
        _TRIU_I = jnp.asarray(_TRIU_I)
        _TRIU_J = jnp.asarray(_TRIU_J)
        combined = jnp.concatenate([sparse_x, dense_x[:, None, :]], axis=1)
        interact = jnp.einsum('bfd,bgd->bfg', combined, combined)
        return interact[:, _TRIU_I, _TRIU_J]
    e = jnp.stack([tbl_0[ids[:, 0]], tbl_1[ids[:, 1]], tbl_2[ids[:, 2]], tbl_3[ids[:, 3]], tbl_4[ids[:, 4]], tbl_5[ids[:, 5]], tbl_6[ids[:, 6]], tbl_7[ids[:, 7]], tbl_8[ids[:, 8]], tbl_9[ids[:, 9]], tbl_10[ids[:, 10]], tbl_11[ids[:, 11]], tbl_12[ids[:, 12]], tbl_13[ids[:, 13]], tbl_14[ids[:, 14]], tbl_15[ids[:, 15]], tbl_16[ids[:, 16]], tbl_17[ids[:, 17]], tbl_18[ids[:, 18]], tbl_19[ids[:, 19]], tbl_20[ids[:, 20]], tbl_21[ids[:, 21]], tbl_22[ids[:, 22]], tbl_23[ids[:, 23]], tbl_24[ids[:, 24]], tbl_25[ids[:, 25]]], axis=1)
    z = _L0_rec_ref(e, r_dense_x)
    z = z.reshape(z.shape[0], -1)
    h = jnp.concatenate([z, r_dense_x], axis=1)
    h = jnp.maximum(h @ W_top1 + b_top1, 0.0)
    h = jnp.maximum(h @ W_top2 + b_top2, 0.0)
    y = h @ W_top3
    return y

_drawn_inputs = setup_inputs


def setup_inputs(seed=0):
    import zlib

    import numpy as np

    out = dict(_drawn_inputs(seed))
    spreads = {'b_top1': (0.0, 0.1), 'b_top2': (0.0, 0.1)}
    factors = {}
    for name, (base, spread) in spreads.items():
        noise = np.random.default_rng([zlib.crc32(name.encode()), seed]).standard_normal(out[name].shape)
        drawn = base * np.exp(spread * noise) if base else spread * noise
        out[name] = jnp.asarray(drawn.astype(out[name].dtype))
    for name, factor in factors.items():
        out[name] = (out[name] * factor).astype(out[name].dtype)
    return out
```

```python
from contextlib import ExitStack

import numpy as np

import concourse.bass as bass
from concourse import mybir
from concourse.alu_op_type import AluOpType as ALU

ACT = mybir.ActivationFunctionType
F32 = mybir.dt.float32
F32R = mybir.dt.float32r
I32 = mybir.dt.int32

P = 128
B = 2048
D = 128
F = 26
TILES = B // P
CT = 2
CHUNKS = TILES // CT
CS = CT * P
Q = 32
QUADS = P // Q

ONE_HOT = [6, 8, 11, 12, 13, 14, 21, 22]
GATHERED = [f for f in range(F) if f not in ONE_HOT]
NO, NG = len(ONE_HOT), len(GATHERED)
ROWS = 1000
KT = 8
RP = ROWS // KT

DENSE = 26
ORDER = GATHERED + [DENSE] + ONE_HOT
NF = F + 1
NROW = NG + 1
GROUP = 4
GROUPS = [list(range(g, min(g + GROUP, NROW))) for g in range(0, NROW, GROUP)]
NGR = len(GROUPS)
GS = NF - 1

PK = (NF - 1) // 2
PAIRS = PK * NF
ZT = [(s, min(P, PAIRS - s)) for s in range(0, PAIRS, P)]
H1, H2 = 512, 256
T1, T2 = H1 // P, H2 // P

OH_RING = 16
UNITS = NO * KT
TR_USES = NO + CT * NGR
RAWS = 4
PARTS = 16
assert UNITS % OH_RING == 0 and PAIRS == NF * (NF - 1) // 2


def build(nc, t_, out):
    ctx = ExitStack()
    with ctx:
        def sb(name, shape, dt=F32):
            return ctx.enter_context(nc.sbuf_tensor(name, shape, dt))

        def pb(name, shape):
            return ctx.enter_context(nc.psum_tensor(name, shape, F32))

        def sem(name):
            return ctx.enter_context(nc.semaphore(name))

        gather_ids = [sb(f"gather_ids{t}", [P, F], I32) for t in range(CT)]
        rows = [sb(f"rows{t}", [P, NROW, D]) for t in range(CT)]
        xt = [sb(f"xt{t}", [P, P, NF]) for t in range(CT)]
        dense_t = [sb(f"dense_t{t}", [P, P]) for t in range(CT)]
        onehot_ids = sb("onehot_ids", [P, NO, CS], I32)
        ids_from = sb("ids_from", [P, NO, CS])
        onehot = sb("onehot", [P, OH_RING, CS], F32R)
        raw = [sb(f"raw{i}", [P, KT, D]) for i in range(RAWS)]
        table = sb("table", [P, NO, 2, KT, D], F32R)
        first_i = sb("first_i", [P, 1], I32)
        first = sb("first", [P, 1])
        ident = sb("ident", [P, P])
        lower = sb("lower", [P, PK, PK])
        zs = sb("zs", [P, GS, Q])
        packed = sb("packed", [P, PK, NF])
        zt = sb("zt", [P, len(ZT), P])
        h1 = sb("h1", [P, T1, P])
        h2 = sb("h2", [P, T2, P])
        w1 = sb("w1", [P, len(ZT) + 1, H1])
        w2 = sb("w2", [P, T1, H2])
        cols = sb("cols", [P, T1 + T2 + T2])
        y = sb("y", [P, TILES])

        ps_tr = [pb(f"ps_tr{i}", [P, 512]) for i in range(2)]
        ps_gram = [pb(f"ps_gram{t}", [P, Q, Q]) for t in range(CT)]
        ps_zt = pb("ps_zt", [P, 512])
        ps_mlp = pb("ps_mlp", [P, 512])
        ps_y = ps_zt[:, len(ZT) * P:len(ZT) * P + 1]

        s_gids = [sem(f"s_gids{t}") for t in range(CT)]
        s_oids = sem("s_oids")
        s_from = sem("s_from")
        s_dense = [sem(f"s_dense{t}") for t in range(CT)]
        s_rows = [[sem(f"s_rows{t}_{g}") for g in range(NGR)] for t in range(CT)]
        s_raw = [sem(f"s_raw{i}") for i in range(RAWS)]
        s_w = sem("s_w")
        s_cols = sem("s_cols")
        s_out = sem("s_out")
        s_ident = sem("s_ident")
        s_const = sem("s_const")
        s_first = sem("s_first")
        s_high = sem("s_high")
        s_low = sem("s_low")
        s_unit = sem("s_unit")
        s_unit_used = sem("s_unit_used")
        s_tr = sem("s_tr")
        s_evac = sem("s_evac")
        s_gram = sem("s_gram")
        s_zero = sem("s_zero")
        s_zs = sem("s_zs")
        s_pack1 = sem("s_pack1")
        s_packed = sem("s_packed")
        s_ztps = sem("s_ztps")
        s_zt = sem("s_zt")
        s_h1ps = sem("s_h1ps")
        s_h1 = sem("s_h1")
        s_h2ps = sem("s_h2ps")
        s_h2 = sem("s_h2")
        s_yps = sem("s_yps")
        s_y = sem("s_y")

        s_carrier = {e: sem(f"s_carrier_{e}") for e in ("dve", "pool", "sp")}

        dense_v = t_["r_dense_x"].rearrange("(p t) d -> p t d", t=TILES)
        ids_v = t_["ids"].rearrange("(p t) f -> p t f", t=TILES)

        def use_of_table(c, j):
            return j if isinstance(c, int) and c == 0 else (c * TR_USES) + (NGR + j)

        def use_of_group(c, t, g):
            return NO + g if t == 0 else (c * TR_USES) + (NO + t * NGR + g)

        def table_bank(c, j):
            return ps_tr[use_of_table(0 if isinstance(c, int) and c == 0 else 2, j) % 2]

        def group_bank(t, g):
            return ps_tr[use_of_group(0, t, g) % 2]

        groups = [f"T{g}" for g in range(NGR)]
        rest = " ".join(groups[4:])
        AFTER_LOOKUP = f"Z T0 3 L1 T1 4 T2 L2 2 T3 L3 3 {rest} 4".split()
        AFTER_GRAM = f"3 T0 4 Z 3 T1 L1 3 T2 3 L2 T3 L3 {rest}".split()
        LAST = "2 Z 6 L1 8 L2 L3".split()

        def schedule(t, mlp, last):
            if last:
                return LAST
            order = AFTER_GRAM if t else AFTER_LOOKUP
            return [w for w in order if w.isdigit() or w[0] == "T" or mlp]

        def tile_of(c, t, what):
            if what[0] == "T":
                return c, t + 1, int(what[1:])
            return (c, t - 1) if t > 0 else (c - 1, CT - 1)

        def row_copies(c, t, g):
            return ((c + t // CT) + 1) * (16 * len([r for r in GROUPS[g] if r < NG]))

        block = ctx.enter_context(nc.Block())

        @block.sync
        def _(sp):
            def load_gather_ids(c, t):
                sp.dma_start(gather_ids[t][:, :], ids_v[:, bass.ds(c * CT + t, 1), :].rearrange("p o f -> p (o f)")
                             ).then_inc(s_gids[t], 16)

            def load_dense(c, t):
                sp.dma_start(rows[t][:, NG, :], dense_v[:, bass.ds(c * CT + t, 1), :].rearrange("p o d -> p (o d)")
                             ).then_inc(s_dense[t], 16)

            def load_onehot_ids(c):
                sp.dma_start(onehot_ids[:, :, :].rearrange("p a s -> p (a s)"),
                             t_["ids_onehot"][bass.ds(c, 1), :].to_broadcast([P, NO * CS])).then_inc(s_oids, 16)

            def ahead(c):
                for t in range(CT):
                    for g in range(NGR):
                        n = len([r for r in GROUPS[g] if r < NG])
                        if n:
                            sp.wait_ge(s_rows[t][g], (c + 1) * (16 * n))
                            sp.sem_inc(s_carrier["sp"], 1)
                    load_gather_ids(c + 1, t)
                    if t == 0:
                        sp.wait_ge(s_from, c + 1)
                        sp.sem_inc(s_carrier["sp"], 1)
                        load_onehot_ids(c + 1)
                    sp.wait_ge(s_tr, (c * CT + (t + 1)) * NGR)
                    sp.sem_inc(s_carrier["sp"], 1)
                    load_dense(c + 1, t)

            for t in range(CT):
                load_gather_ids(0, t)
            for j, f in enumerate(ONE_HOT):
                if j >= RAWS:
                    sp.wait_ge(s_low, j - RAWS + 1)
                sp.dma_start(raw[j % RAWS][0:RP, :, :], t_[f"tbl_{f}"].rearrange("(p k) d -> p k d", k=KT)
                             ).then_inc(s_raw[j % RAWS], 16)
                if j == 0:
                    load_onehot_ids(0)
                    sp.dma_start(cols[:, :], t_["cols"]).then_inc(s_cols, 16)
            for t in range(CT):
                load_dense(0, t)
            full = sum(n == P for _, n in ZT)
            sp.dma_start(w1[:, 0:full, :], t_["w1"][0:full * P, :].rearrange("(k p) n -> p k n", p=P)).then_inc(s_w, 16)
            sp.dma_start(w1[0:ZT[-1][1], full, :], t_["w1"][full * P:PAIRS, :]).then_inc(s_w, 16)
            sp.dma_start(w1[:, len(ZT), :], t_["w1"][PAIRS:PAIRS + D, :]).then_inc(s_w, 16)
            sp.dma_start(w2[:, :, :], t_["W_top2"].rearrange("(k p) n -> p k n", p=P)).then_inc(s_w, 16)
            ahead(0)
            with sp.Fori(1, CHUNKS - 1) as c:
                ahead(c)
            sp.wait_ge(s_y, TILES)
            sp.dma_start(out.rearrange("(p t) o -> p (t o)", t=TILES), y[:, :]).then_inc(s_out, 16)
            sp.wait_ge(s_out, 16)

        @block.gpsimd
        def _(pool):
            def gather(c):
                for t in range(CT):
                    pool.wait_ge(s_gids[t], (c + 1) * 16)
                    if not isinstance(c, int) or c > 0:
                        pool.wait_ge(s_tr, ((c - 1) * CT + (t + 1)) * NGR)
                    pool.sem_inc(s_carrier["pool"], 1)
                    for r, f in enumerate(GATHERED):
                        pool.indirect_dma_start(
                            rows[t][:, r, :], None, t_[f"tbl_{f}"],
                            bass.IndirectOffsetOnAxis(ap=gather_ids[t][:, f:f + 1], axis=0)
                        ).then_inc(s_rows[t][r // GROUP], 16)

            pool.iota(first_i[:, :], pattern=[[0, 1]], base=0, channel_multiplier=-KT).then_inc(s_const, 1)
            pool.memset(ident[:, :], 0.0).then_inc(s_ident, 1)
            pool.memset(lower[:, :, :], 1.0).then_inc(s_const, 1)
            pool.wait_ge(s_ident, 1)
            pool.affine_select(out=ident[:, :], in_=ident[:, :], compare_op=ALU.not_equal, fill=1.0,
                               base=0, pattern=[[-1, P]], channel_multiplier=1).then_inc(s_ident, 1)
            pool.wait_ge(s_const, 2)
            pool.affine_select(out=lower[:, :, :], in_=lower[:, :, :], compare_op=ALU.is_gt, fill=0.0,
                               base=1, pattern=[[1, PK], [-1, PK]], channel_multiplier=0).then_inc(s_const, 1)
            gather(0)
            with pool.Fori(1, CHUNKS) as c:
                gather(c)

        @block.vector
        def _(dve):
            def make_units(c, lo, hi):
                for u in range(lo, hi):
                    j, k = divmod(u, KT)
                    if not isinstance(c, int) or c > 0:
                        dve.wait_ge(s_unit_used, (c - 1) * UNITS + (UNITS + u - OH_RING + 1))
                    elif u >= OH_RING:
                        dve.wait_ge(s_unit_used, u - OH_RING + 1)
                    nc.vector.tensor_scalar(onehot[0:RP, u % OH_RING, :], ids_from[0:RP, j, :],
                                            float(k), None, ALU.is_equal).then_inc(s_unit, 1)

            def units_start(c):
                dve.wait_ge(s_from, c + 1)
                make_units(c, 0, OH_RING)

            def pack(c, t):
                dve.wait_ge(s_gram, c * CT + (t + 1))
                nc.vector.transpose(zs[:, :, :], ps_gram[t][:, :, 0:GS].rearrange("p s g -> p g s")).then_inc(s_zs, 1)
                dve.wait_ge(s_zs, c * CT + (t + 1))
                if t > 0 or not isinstance(c, int) or c > 0:
                    dve.wait_ge(s_ztps, c * CT + t)
                nc.vector.tensor_copy(packed[:, :, :], zs[:, GS - 1:GS - 1 - PK:-1, NF - 1::-1][:, :, 0:NF]
                                      ).then_inc(s_pack1, 1)
                dve.wait_ge(s_pack1, c * CT + (t + 1))
                dve.sem_inc(s_carrier["dve"], 1)
                nc.vector.copy_predicated(packed[:, :, 0:PK], lower[:, :, :].bitcast(I32), zs[:, 0:PK, 0:PK]
                                          ).then_inc(s_packed, 1)

            for t in range(CT):
                nc.vector.memset(ps_gram[t][:, :, :], 0.0).then_inc(s_zero, 1)
            dve.wait_ge(s_const, 1)
            nc.vector.tensor_copy(first[:, :], first_i[:, :]).then_inc(s_first, 1)
            for j in range(NO):
                dve.wait_ge(s_high, j + 1)
                nc.vector.tensor_tensor(table[0:RP, j, 1, :, :], raw[j % RAWS][0:RP, :, :],
                                        table[0:RP, j, 0, :, :].bitcast(F32), ALU.subtract).then_inc(s_low, 1)
                if j == 0:
                    dve.wait_ge(s_from, 1)
                make_units(0, j * KT, (j + 1) * KT)
            dve.wait_ge(s_const, 3)
            pack(0, 0)
            units_start(1)

            def chunk(c):
                pack(c - 1, CT - 1)
                make_units(c, OH_RING, UNITS)
                for t in range(CT - 1):
                    pack(c, t)

            with dve.Fori(1, CHUNKS - 1) as c:
                chunk(c)
                units_start(c + 1)
            chunk(CHUNKS - 1)
            pack(CHUNKS - 1, CT - 1)

        @block.scalar
        def _(act):
            def evac_table(c, j):
                act.wait_ge(s_unit_used, c * UNITS + (j + 1) * KT)
                if j == 0 and (not isinstance(c, int) or c > 0):
                    act.wait_ge(s_gram, c * CT)
                for t in range(CT):
                    i = nc.scalar.copy(xt[t][:, :, NROW + j], table_bank(c, j)[:, t * P:(t + 1) * P])
                i.then_inc(s_evac, 1)

            def evac_tables(c):
                for j in range(NO):
                    evac_table(c, j)

            def shift_ids(c):
                act.wait_ge(s_oids, (c + 1) * 16)
                if not isinstance(c, int) or c > 0:
                    act.wait_ge(s_unit, c * UNITS)
                nc.scalar.activation(ids_from[0:RP, :, :], onehot_ids[0:RP, :, :], ACT.Identity,
                                     bias=first[0:RP, :]).then_inc(s_from, 1)

            def evac_group(c, t, g):
                act.wait_ge(s_tr, (c * CT + t) * NGR + (g + 1))
                if g == 0 and (t >= CT or not isinstance(c, int) or c > 0):
                    act.wait_ge(s_gram, c * CT + (t - CT + 1))
                n, a = len(GROUPS[g]), GROUPS[g][0]
                bank, x = group_bank(t, g), xt[t % CT]
                if NG in GROUPS[g]:
                    k = GROUPS[g].index(NG)
                    nc.scalar.copy(dense_t[t % CT][:, :], bank[:, k * P:(k + 1) * P])
                nc.scalar.copy(x[:, :, a:a + n].rearrange("p s f -> p f s"),
                               bank[:, 0:n * P].rearrange("p (f s) -> p f s", f=n)).then_inc(s_evac, 1)

            def evac_zt(c, t):
                act.wait_ge(s_ztps, c * CT + (t + 1))
                full = sum(n == P for _, n in ZT)
                nc.scalar.copy(zt[:, 0:full, :].rearrange("p k s -> p (k s)"), ps_zt[:, 0:full * P])
                nc.scalar.copy(zt[0:ZT[-1][1], full, :], ps_zt[0:ZT[-1][1], full * P:(full + 1) * P]).then_inc(s_zt, 1)

            def relu1(c, t):
                act.wait_ge(s_h1ps, c * CT + (t + 1))
                for j in range(T1):
                    i = nc.scalar.activation(h1[:, j, :], ps_mlp[:, j * P:(j + 1) * P], ACT.Relu,
                                             bias=cols[:, j:j + 1])
                i.then_inc(s_h1, 1)

            def relu2(c, t):
                act.wait_ge(s_h2ps, c * CT + (t + 1))
                for j in range(T2):
                    i = nc.scalar.activation(h2[:, j, :], ps_mlp[:, j * P:(j + 1) * P], ACT.Relu,
                                             bias=cols[:, T1 + j:T1 + j + 1])
                i.then_inc(s_h2, 1)

            def keep_y(c, t):
                act.wait_ge(s_yps, c * CT + (t + 1))
                nc.scalar.copy(y[:, bass.ds(c * CT + t, 1)], ps_y).then_inc(s_y, 1)

            work = {"Z": evac_zt, "L1": relu1, "L2": relu2, "L3": keep_y, "T": evac_group}

            def do(c, t, what):
                work[what.rstrip("01234") if what[0] == "T" else what](*tile_of(c, t, what))

            def step(c, t, mlp=True, last=False):
                for what in schedule(t, mlp, last):
                    if not what.isdigit():
                        do(c, t, what)

            def high(j):
                act.wait_ge(s_raw[j % RAWS], 16 * (j // RAWS + 1))
                nc.scalar.copy(table[0:RP, j, 0, :, :], raw[j % RAWS][0:RP, :, :]).then_inc(s_high, 1)

            high(0)
            act.wait_ge(s_first, 1)
            shift_ids(0)
            for j in range(1, min(RAWS, NO)):
                high(j)
            act.wait_ge(s_cols, 16)
            for j in range(NO):
                evac_table(0, j)
                if j + RAWS < NO:
                    high(j + RAWS)
            for g in range(NGR):
                evac_group(0, 0, g)
            step(0, 0, mlp=False)
            shift_ids(1)
            step(0, 1)
            with act.Fori(1, CHUNKS - 1) as c:
                evac_tables(c)
                step(c, 0)
                shift_ids(c + 1)
                step(c, 1)
            evac_tables(CHUNKS - 1)
            step(CHUNKS - 1, 0)
            step(CHUNKS - 1, CT - 1, last=True)
            for what in ("Z", "L1", "L2", "L3"):
                work[what](CHUNKS - 1, CT - 1)

        @block.tensor
        def _(pe):
            def bank_free(use):
                if not isinstance(use, int) or use >= 2:
                    pe.wait_ge(s_evac, use - 1)

            def lookup(c):
                for j in range(NO):
                    bank_free(use_of_table(c, j))
                    for k in range(KT):
                        pe.wait_ge(s_unit, c * UNITS + (j * KT + k + 1))
                        if isinstance(c, int) and c == 0 and k == 0:
                            pe.wait_ge(s_low, j + 1)
                        for part in range(2):
                            i = nc.tensor.matmul(table_bank(c, j)[:, 0:CS], table[0:RP, j, part, k, :],
                                                 onehot[0:RP, (j * KT + k) % OH_RING, :],
                                                 start=(k == 0 and part == 0), stop=(k == KT - 1 and part == 1))
                        i.then_inc(s_unit_used, 1)

            def turn(c, t, g):
                bank_free(use_of_group(c, t, g))
                if any(r < NG for r in GROUPS[g]):
                    pe.wait_ge(s_rows[t % CT][g], row_copies(c, t, g))
                if NG in GROUPS[g]:
                    pe.wait_ge(s_dense[t % CT], ((c + t // CT) + 1) * 16)
                for k, r in enumerate(GROUPS[g]):
                    i = nc.tensor.transpose(group_bank(t, g)[:, k * P:(k + 1) * P], rows[t % CT][:, r, :], ident[:, :])
                i.then_inc(s_tr, 1)

            def gram(c, t, lo, hi):
                if lo == 0:
                    pe.wait_ge(s_evac, use_of_group(c, t + 1, 0))
                    if not isinstance(c, int) or c > 0:
                        pe.wait_ge(s_zs, (c - 1) * CT + (t + 1))
                    else:
                        pe.wait_ge(s_zero, CT)
                for s in range(lo, hi):
                    for q in range(QUADS):
                        i = nc.tensor.matmul(ps_gram[t][q * Q:q * Q + GS, s, 0:GS], xt[t][:, q * Q + s, 0:GS],
                                             xt[t][:, q * Q + s, 1:NF], start=True, stop=True)
                if hi == Q:
                    i.then_inc(s_gram, 1)

            def turn_pairs(c, t):
                pe.wait_ge(s_packed, c * CT + (t + 1))
                if t > 0 or not isinstance(c, int) or c > 0:
                    pe.wait_ge(s_y, c * CT + t)
                flat = packed[:, :, :].rearrange("p k i -> p (k i)")
                for k, (a, n) in enumerate(ZT):
                    i = nc.tensor.transpose(ps_zt[0:n, k * P:(k + 1) * P], flat[:, a:a + n], ident[:, :])
                i.then_inc(s_ztps, 1)

            def layer1(c, t):
                pe.wait_ge(s_zt, c * CT + (t + 1))
                if t > 0 or not isinstance(c, int) or c > 0:
                    pe.wait_ge(s_h2, c * CT + t)
                else:
                    pe.wait_ge(s_w, 16 * 4)
                for j in range(T1):
                    for k in range(len(ZT) + 1):
                        n = ZT[k][1] if k < len(ZT) else D
                        x = zt[0:n, k, :] if k < len(ZT) else dense_t[t][:, :]
                        i = nc.tensor.matmul(ps_mlp[:, j * P:(j + 1) * P], w1[0:n, k, j * P:(j + 1) * P], x,
                                             start=(k == 0), stop=(k == len(ZT)))
                i.then_inc(s_h1ps, 1)

            def layer2(c, t):
                pe.wait_ge(s_h1, c * CT + (t + 1))
                for j in range(T2):
                    for k in range(T1):
                        i = nc.tensor.matmul(ps_mlp[:, j * P:(j + 1) * P], w2[:, k, j * P:(j + 1) * P], h1[:, k, :],
                                             start=(k == 0), stop=(k == T1 - 1))
                i.then_inc(s_h2ps, 1)

            def layer3(c, t):
                pe.wait_ge(s_h2, c * CT + (t + 1))
                for k in range(T2):
                    i = nc.tensor.matmul(ps_y, h2[:, k, :], cols[:, T1 + T2 + k:T1 + T2 + k + 1],
                                         start=(k == 0), stop=(k == T2 - 1))
                i.then_inc(s_yps, 1)

            work = {"Z": turn_pairs, "L1": layer1, "L2": layer2, "L3": layer3, "T": turn}

            def do(c, t, what):
                work[what.rstrip("01234") if what[0] == "T" else what](*tile_of(c, t, what))

            def step(c, t, mlp=True, last=False):
                done = 0
                for what in schedule(t, mlp, last):
                    if what.isdigit():
                        gram(c, t, done, done + int(what) * (Q // PARTS))
                        done += int(what) * (Q // PARTS)
                    else:
                        do(c, t, what)
                assert done == Q

            pe.wait_ge(s_ident, 2)
            pe.wait_ge(s_cols, 16)
            lookup(0)
            for g in range(NGR):
                turn(0, 0, g)
            step(0, 0, mlp=False)
            step(0, 1)
            with pe.Fori(1, CHUNKS - 1) as c:
                lookup(c)
                step(c, 0)
                step(c, 1)
            lookup(CHUNKS - 1)
            step(CHUNKS - 1, 0)
            step(CHUNKS - 1, CT - 1, last=True)
            for what in ("Z", "L1", "L2", "L3"):
                work[what](CHUNKS - 1, CT - 1)


def pair_row(a, b):
    f, g = min(a, b), max(a, b)
    return f * NF - f * (f + 1) // 2 + (g - f - 1)


def kernel(**inputs):
    import concourse.bacc as bacc
    from concourse.bass_utils import run_bass_kernel_spmd

    nc = bacc.Bacc("TRN2", target_bir_lowering=False, num_devices=1)
    x = {name: np.ascontiguousarray(a) for name, a in inputs.items()}

    slots = [(i, k) if i < k else (NF - 1 - i, NF - k) for k in range(1, PK + 1) for i in range(NF)]
    perm = [pair_row(ORDER[f], ORDER[g]) for f, g in slots] + list(range(PAIRS, PAIRS + D))
    arrays = {name: x[name] for name in ["r_dense_x", "ids", "W_top2"] + [f"tbl_{f}" for f in range(F)]}
    arrays["w1"] = x["W_top1"][perm]
    arrays["cols"] = np.ascontiguousarray(np.concatenate(
        [x["b_top1"].reshape(T1, P), x["b_top2"].reshape(T2, P), x["W_top3"].reshape(T2, P)]).T)
    ids = x["ids"].reshape(P, CHUNKS, CT, F)[:, :, :, ONE_HOT]
    arrays["ids_onehot"] = np.ascontiguousarray(ids.transpose(1, 3, 2, 0)).reshape(CHUNKS, NO * CS)

    t_ = {n: nc.dram_tensor(f"in_{n}", a.shape, mybir.dt.from_np(a.dtype), kind="ExternalInput").ap()
          for n, a in arrays.items()}
    out = nc.dram_tensor("out_y", (B, 1), F32, kind="ExternalOutput").ap()
    build(nc, t_, out)
    r = run_bass_kernel_spmd(nc, [{f"in_{n}": a for n, a in arrays.items()}], core_ids=[0])
    return r.results[0]["out_y"]
```
